# Optimizing a Trainium2 kernel written in Bass

```python
import numpy as np
import jax
import jax.numpy as jnp

def _softmax(x, axis=-1):
    return jax.nn.softmax(x, axis=axis)

def _gelu(x):
    return jax.nn.gelu(x, approximate=True)

def _silu(x):
    return jax.nn.silu(x)

def _sigmoid(x):
    return jax.nn.sigmoid(x)

def _layernorm(x, axis=-1, eps=1e-05):
    m = jnp.mean(x, axis=axis, keepdims=True)
    v = jnp.var(x, axis=axis, keepdims=True)
    return (x - m) / jnp.sqrt(v + eps)

def _scatter_add(tgt, idx, src, axis=0):
    return tgt.at[idx].add(src)

def _segment_sum(src, seg, n):
    return jax.ops.segment_sum(src, seg, n)
kernel_name = 'mk_cond_resid_d2_seqx_r2_5f345b'

def setup_inputs(seed: int=0):
    np.random.seed(seed)
    _w = jnp.asarray

    def _rec_inputs():
        import jax
        import jax.numpy as jnp
        _rk = jax.random.key(seed)
        x = -7.109e-05 + 0.9999 * jax.random.normal(jax.random.fold_in(_rk, 1), (128, 128, 1024), jnp.float32)
        _lenS = 128 - jax.random.randint(jax.random.fold_in(_rk, 7), (128,), 0, max(1, 128 // 4) + 1, jnp.int32)
        _lenS2 = 128 - jax.random.randint(jax.random.fold_in(_rk, 8), (128,), 0, max(1, 128 // 4) + 1, jnp.int32)
        itok_B_1_198 = jax.random.randint(jax.random.fold_in(_rk, 11), (128,), 1, 199, jnp.int32)
        itok_B_0_6 = jax.random.randint(jax.random.fold_in(_rk, 12), (128,), 0, 7, jnp.int32)
        return (x, itok_B_1_198, itok_B_0_6)
    x, itok_B_1_198, itok_B_0_6 = _rec_inputs()

    def _L0_cond_setup():
        import jax, jax.numpy as jnp
        import numpy as np
        B, C, T = (128, 128, 1024)
        S, D = (200, 128)
        key = jax.random.key(seed)
        k1, k2, k3 = jax.random.split(key, 3)
        x = jax.random.normal(k1, (B, C, T), dtype=jnp.float32)
        conditions = jax.random.randint(k2, (B,), 0, S, dtype=jnp.int64)
        weights = jax.random.normal(k3, (S, C, D), dtype=jnp.float32) / jnp.sqrt(jnp.float32(C))
        return {'x': x, 'conditions': conditions, 'weights': weights}
    _L0_cond_all = _L0_cond_setup()
    _L0_cond_in = {k: v for k, v in _L0_cond_all.items() if k in ('weights',)}
    del _L0_cond_all

    def _L1_cond_setup():
        import jax, jax.numpy as jnp
        import numpy as np
        B, T, D_IN, D_OUT = (16, 1024, 1024, 1024)
        N_ADAPTERS, RANK = (8, 16)
        key = jax.random.key(seed)
        k_x, k_w, k_a, k_b, k_s, k_idx = jax.random.split(key, 6)
        x = jax.random.normal(k_x, (B, T, D_IN), dtype=jnp.float32)
        W = jax.random.normal(k_w, (D_OUT, D_IN), dtype=jnp.float32) * (1.0 / np.sqrt(D_IN))
        A = jax.random.normal(k_a, (N_ADAPTERS, RANK, D_IN), dtype=jnp.float32) * 0.02
        Bm = jax.random.normal(k_b, (N_ADAPTERS, D_OUT, RANK), dtype=jnp.float32) * 0.02
        scalings = jnp.ones((N_ADAPTERS,), dtype=jnp.float32)
        adapter_idx = jax.random.randint(k_idx, (B,), 0, N_ADAPTERS, dtype=jnp.int32)
        return {'x': x, 'W': W, 'A': A, 'Bm': Bm, 'scalings': scalings, 'adapter_idx': adapter_idx}
    _L1_cond_all = _L1_cond_setup()
    _L1_cond_in = {k: v for k, v in _L1_cond_all.items() if k in ('W', 'A', 'Bm', 'scalings')}
    del _L1_cond_all
    return {'x': x, 'itok_B_1_198': itok_B_1_198, 'itok_B_0_6': itok_B_0_6, 'L0_cond_weights': _L0_cond_in['weights'], 'L1_cond_W': _L1_cond_in['W'], 'L1_cond_A': _L1_cond_in['A'], 'L1_cond_Bm': _L1_cond_in['Bm'], 'L1_cond_scalings': _L1_cond_in['scalings']}

def reference(x, itok_B_1_198, itok_B_0_6, L0_cond_weights, L1_cond_W, L1_cond_A, L1_cond_Bm, L1_cond_scalings):
    import jax
    import jax.numpy as jnp

    def _L0_cond_ref(x, conditions, weights):
        import jax, jax.numpy as jnp
        import numpy as np
        B, C, T = (128, 128, 1024)
        S, D = (200, 128)
        w = weights[conditions]
        return jnp.einsum('bct,bcd->bdt', x, w)

    def _L1_cond_ref(x, W, A, Bm, scalings, adapter_idx):
        import jax, jax.numpy as jnp
        import numpy as np
        B, T, D_IN, D_OUT = (16, 1024, 1024, 1024)
        N_ADAPTERS, RANK = (8, 16)
        H = jnp.einsum('btd,od->bto', x, W)
        A_b = A[adapter_idx]
        B_b = Bm[adapter_idx]
        s_b = scalings[adapter_idx]
        xa = jnp.einsum('btd,brd->btr', x, A_b)
        delta = jnp.einsum('btr,bor->bto', xa, B_b)
        delta = jax.lax.stop_gradient(delta * s_b[:, None, None])
        return H + delta
    x = x + _L0_cond_ref(x, itok_B_1_198, L0_cond_weights)
    x = x + _L1_cond_ref(x, L1_cond_W, L1_cond_A, L1_cond_Bm, L1_cond_scalings, itok_B_0_6)
    return x

_drawn_inputs = setup_inputs


def setup_inputs(seed=0):
    import zlib

    import numpy as np

    out = dict(_drawn_inputs(seed))
    spreads = {'L1_cond_scalings': (1.0, 0.2)}
    factors = {}
    for name, (base, spread) in spreads.items():
        noise = np.random.default_rng([zlib.crc32(name.encode()), seed]).standard_normal(out[name].shape)
        drawn = base * np.exp(spread * noise) if base else spread * noise
        out[name] = jnp.asarray(drawn.astype(out[name].dtype))
    for name, factor in factors.items():
        out[name] = (out[name] * factor).astype(out[name].dtype)
    return out
```

```python
from contextlib import ExitStack

import concourse.bass as bass
from concourse import mybir

F32 = mybir.dt.float32
F32R = mybir.dt.float32r
I32 = mybir.dt.int32
ALU = mybir.AluOpType
ACT = mybir.ActivationFunctionType

P = 128
SLOTS = 2


def bass_cond_then_lora(nc: bass.Bass, x, cond, adapter, cond_w, w_t, a_t, b_t, scalings, out):
    B, C, T = x.shape
    n_cond, _, D = cond_w.shape
    O = w_t.shape[1]
    R, NA, _ = b_t.shape
    K = T // P
    HALF = T // 2
    HK = K // 2
    assert C == P and D == P and T == K * P and O == T and R == 16 and NA * R == P and B % 2 == 0

    ROW = R + O + R
    A_COLS = (0, R + O)
    EVEN = ((0, 348), (348, 348), (696, 344))
    ODD = ((R, 348), (R + 348, 348), (R + 696, 344))
    PIECES = (EVEN, ODD)
    STEP = 32
    WST = 4

    def output_piece(slot, j):
        first, width = PIECES[slot][j]
        lo, hi = max(first, R), min(first + width, R + O)
        return lo - first, lo - R, hi - lo

    xa_bank = (0, 2)
    xa_at = tuple(A_COLS[s] - PIECES[s][xa_bank[s]][0] for s in range(2))

    with ExitStack() as ctx:
        def sb(name, shape, dt):
            return ctx.enter_context(nc.sbuf_tensor(name, shape, dt))

        def sem(name):
            return ctx.enter_context(nc.semaphore(name))

        x_sb = [sb(f"x_sb{s}", [P, T], F32) for s in range(SLOTS)]
        wc_sb = [sb(f"wc_sb{s}", [P, D], F32) for s in range(SLOTS)]
        x1t_hi = [sb(f"x1t_hi{s}", [P, T], F32R) for s in range(SLOTS)]
        x1t_lo = [sb(f"x1t_lo{s}", [P, T], F32R) for s in range(SLOTS)]
        out_sb = [sb(f"out_sb{s}", [P, O], F32) for s in range(SLOTS)]
        w_parts = sb("w_parts", [P, 2 * K, ROW], F32R)
        a_parts = sb("a_parts", [P, 2 * K, P], F32R)
        a_raw = sb("a_raw", [P, K, P], F32)
        w_raw = sb("w_raw", [P, WST, O], F32)
        b_raw = sb("b_raw", [P, NA, O], F32)
        b_stack = sb("b_stack", [P, NA, O], F32R)
        scal = sb("scal", [P, NA], F32)
        low_rows = sb("low_rows", [P, 1], F32)
        ident = sb("ident", [P, P], F32)
        ident_r = sb("ident_r", [P, P], F32R)
        xa_parts = sb("xa_parts", [P, P], F32R)
        xa_t = sb("xa_t", [P, P], F32R)
        cond_sb = sb("cond_sb", [1, B], I32)
        adapter_sb = sb("adapter_sb", [1, B], I32)

        acc = [[ctx.enter_context(nc.psum_tensor(f"acc{s}_{j}", [P, 512], F32)) for j in range(3)] for s in range(2)]
        x1_ps = [ctx.enter_context(nc.psum_tensor(f"x1_ps{h}", [P, HALF], F32)) for h in range(2)]

        idx_loaded = sem("idx_loaded")
        x_loaded = [sem(f"x_loaded{s}") for s in range(SLOTS)]
        wc_loaded = [sem(f"wc_loaded{s}") for s in range(SLOTS)]
        stored = [sem(f"stored{s}") for s in range(SLOTS)]
        w_loaded = [sem(f"w_loaded{k}") for k in range(K)]
        a_loaded = sem("a_loaded")
        b_loaded = sem("b_loaded")
        zeros_set = sem("zeros_set")
        low_rows_set = sem("low_rows_set")
        ident_ready = sem("ident_ready")
        ident_r_ready = sem("ident_r_ready")
        b_cleared = sem("b_cleared")
        w_eye_added = sem("w_eye_added")
        w_hi_ready = sem("w_hi_ready")
        w_lo_ready = sem("w_lo_ready")
        a_hi_ready = sem("a_hi_ready")
        a_lo_ready = sem("a_lo_ready")
        b_scaled = sem("b_scaled")
        b_rounded = sem("b_rounded")
        b_ready = sem("b_ready")
        xa_cleared = sem("xa_cleared")
        wc_ready = sem("wc_ready")
        a_slot_ready = sem("a_slot_ready")
        x1_done = sem("x1_done")
        x1_hi_ready = sem("x1_hi_ready")
        x1_lo_ready = sem("x1_lo_ready")
        main_done = sem("main_done")
        xa_hi_ready = sem("xa_hi_ready")
        xa_ready = sem("xa_ready")
        xa_turned = sem("xa_turned")
        xa_t_ready = sem("xa_t_ready")
        delta_done = sem("delta_done")
        out_act_ready = sem("out_act_ready")
        out_dve_ready = sem("out_dve_ready")

        block = ctx.enter_context(nc.Block())

        def is_first(b):
            return isinstance(b, int) and b == 0

        def is_last(b):
            return isinstance(b, int) and b == B - 1

        @block.sync
        def _(sp):
            def load_x(b, slot):
                sp.dma_start(x_sb[slot][:, :], x[bass.ds(b, 1), :, :].rearrange("b c t -> (b c) t")
                             ).then_inc(x_loaded[slot], 16)

            def load_wc(b, slot):
                c = sp.value_load(cond_sb[0:1, bass.ds(b, 1)], min_val=0, max_val=n_cond - 1)
                sp.dma_start(wc_sb[slot][:, :], cond_w[bass.ds(c, 1), :, :].rearrange("s c d -> (s c) d")
                             ).then_inc(wc_loaded[slot], 16)

            sp.dma_start(cond_sb[:, :], cond).then_inc(idx_loaded, 16)
            sp.dma_start(adapter_sb[:, :], adapter).then_inc(idx_loaded, 16)
            load_x(0, 0)
            sp.wait_ge(idx_loaded, 32)
            load_wc(0, 0)
            for k in range(WST):
                sp.dma_start(w_raw[:, k, :], w_t[k * P:(k + 1) * P, :]).then_inc(w_loaded[k], 16)
                if k == 0:
                    sp.dma_start(a_raw[:, :, :], a_t.rearrange("(k p) m -> p k m", p=P)).then_inc(a_loaded, 16)
            for k in range(WST, K):
                sp.wait_ge(w_lo_ready, k - WST + 1)
                sp.dma_start(w_raw[:, k % WST, :], w_t[k * P:(k + 1) * P, :]).then_inc(w_loaded[k], 16)
            load_x(1, 1)
            load_wc(1, 1)
            sp.wait_ge(b_cleared, NA)
            for g in range(P // STEP):
                sp.dma_start(b_raw[g * STEP:g * STEP + R, :, :], b_t).then_inc(b_loaded, 16)
            sp.dma_start(scal[:, :], scalings.to_broadcast([P, NA])).then_inc(b_loaded, 16)

            def store(b, slot):
                sp.wait_ge(out_act_ready, b + 1)
                sp.wait_ge(out_dve_ready, b + 1)
                sp.dma_start(out[bass.ds(b, 1), :, :].rearrange("b c t -> (b c) t"), out_sb[slot][:, :]
                             ).then_inc(stored[slot], 16)

            def step(b, slot):
                if not is_last(b):
                    sp.wait_ge(x1_done, 2 * b + 2)
                    load_x(b + 2, slot)
                    load_wc(b + 2, slot)
                if not is_first(b):
                    store(b - 1, 1 - slot)

            step(0, 0)
            with sp.Fori(0, (B - 4) // 2) as i:
                step(2 * i + 1, 1)
                step(2 * i + 2, 0)
            step(B - 3, 1)
            store(B - 3, 1)
            store(B - 2, 0)
            store(B - 1, 1)
            for s in range(SLOTS):
                sp.wait_ge(stored[s], 16 * (B // 2))

        @block.tensor
        def _(pe):
            def first_product(b, slot, nth):
                pe.wait_ge(x_loaded[slot], 16 * (nth + 1))
                pe.wait_ge(wc_ready, b + 1)
                for h in range(2):
                    for k in range(HK):
                        t0 = (h * HK + k) * P
                        mm = nc.tensor.matmul(x1_ps[h][:, k * P:(k + 1) * P], x_sb[slot][:, t0:t0 + P],
                                              wc_sb[slot][:, :], start=True, stop=True)
                    mm.then_inc(x1_done, 1)

            def second_product(slot, k):
                t = slice(k * P, (k + 1) * P)
                for lhs, part, first in ((x1t_hi, 0, True), (x1t_hi, K, False), (x1t_lo, 0, False)):
                    for j, (c0, width) in enumerate(PIECES[slot]):
                        mm = nc.tensor.matmul(acc[slot][j][:, 0:width], lhs[slot][:, t],
                                              w_parts[:, part + k, c0:c0 + width],
                                              start=(k == 0 and first), stop=False, skip_group_check=True)
                return mm

            def turn_xa(b):
                pe.wait_ge(xa_ready, b + 1)
                nc.tensor.transpose(x1_ps[0][:, 0:P].bitcast(F32R), xa_parts[:, :], ident_r[:, :]
                                    ).then_inc(xa_turned, 1)

            def low_rank_product(b, slot):
                a = pe.value_load(adapter_sb[0:1, bass.ds(b, 1)], min_val=0, max_val=NA - 1)
                pe.wait_ge(xa_t_ready, b + 1)
                for j in range(3):
                    at, o0, width = output_piece(slot, j)
                    rhs = b_stack[:, bass.ds(a, 1), o0:o0 + width].rearrange("p a o -> p (a o)")
                    mm = nc.tensor.matmul(acc[slot][j][:, at:at + width], xa_t[:, :], rhs,
                                          start=False, stop=True, skip_group_check=True)
                mm.then_inc(delta_done, 1)

            def step(b, slot, nth_next):
                pe.wait_ge(a_slot_ready, b + 1)
                if not (isinstance(b, int) and b < 2):
                    pe.wait_ge(out_act_ready, b - 1)
                    pe.wait_ge(out_dve_ready, b - 1)
                for k in range(K):
                    if k % HK == 0:
                        pe.wait_ge(x1_hi_ready, 2 * b + k // HK + 1)
                        pe.wait_ge(x1_lo_ready, 2 * b + k // HK + 1)
                    if is_first(b):
                        pe.wait_ge(w_hi_ready, k + 1)
                        pe.wait_ge(w_lo_ready, k + 1)
                    mm = second_product(slot, k)
                    if k == 0 and not is_first(b):
                        turn_xa(b - 1)
                    if k == 2 and not is_first(b):
                        low_rank_product(b - 1, 1 - slot)
                    if k == HK and not is_last(b):
                        first_product(b + 1, 1 - slot, nth_next)
                mm.then_inc(main_done, 1)

            pe.wait_ge(idx_loaded, 32)
            first_product(0, 0, 0)
            pe.wait_ge(ident_r_ready, 1)
            step(0, 0, 0)
            pe.wait_ge(b_ready, NA)
            step(1, 1, 1)
            with pe.Fori(1, B // 2 - 1) as i:
                step(2 * i, 0, i)
                step(2 * i + 1, 1, i + 1)
            step(B - 2, 0, B // 2 - 1)
            step(B - 1, 1, None)
            turn_xa(B - 1)
            low_rank_product(B - 1, 1)

        @block.scalar
        def _(act):
            act.wait_ge(ident_ready, 1)
            nc.scalar.copy(ident_r[:, :], ident[:, :]).then_inc(ident_r_ready, 1)

            def x1_high(b, slot):
                for h in range(2):
                    act.wait_ge(x1_done, 2 * b + h + 1)
                    nc.scalar.copy(x1t_hi[slot][:, h * HALF:(h + 1) * HALF], x1_ps[h][:, :]).then_inc(x1_hi_ready, 1)

            def finish(b, slot, nth):
                act.wait_ge(xa_turned, b + 1)
                nc.scalar.copy(xa_t[:, :], x1_ps[0][:, 0:P]).then_inc(xa_t_ready, 1)
                act.wait_ge(delta_done, b + 1)
                if nth is not None:
                    act.wait_ge(stored[slot], 16 * nth)
                for j in range(2):
                    at, o0, width = output_piece(slot, j)
                    cp = nc.scalar.copy(out_sb[slot][:, o0:o0 + width], acc[slot][j][:, at:at + width])
                cp.then_inc(out_act_ready, 1)

            x1_high(0, 0)
            for k in range(K):
                act.wait_ge(w_eye_added, k + 1)
                nc.scalar.copy(w_parts[:, k, R:R + O], w_raw[:, k % WST, :]).then_inc(w_hi_ready, 1)
                if k == 0:
                    act.wait_ge(a_loaded, 16)
                    nc.scalar.copy(a_parts[:, 0:K, :], a_raw[:, :, :]).then_inc(a_hi_ready, 1)
            x1_high(1, 1)
            for a in range(NA):
                act.wait_ge(b_scaled, a + 1)
                nc.scalar.copy(b_stack[:, a, :], b_raw[:, a, :]).then_inc(b_rounded, 1)
            finish(0, 0, None)
            x1_high(2, 0)
            finish(1, 1, None)
            x1_high(3, 1)
            with act.Fori(0, (B - 4) // 2) as i:
                finish(2 * i + 2, 0, i + 1)
                x1_high(2 * i + 4, 0)
                finish(2 * i + 3, 1, i + 1)
                x1_high(2 * i + 5, 1)
            finish(B - 2, 0, B // 2 - 1)
            finish(B - 1, 1, B // 2 - 1)

        @block.vector
        def _(dve):
            nc.vector.memset(xa_parts[:, :].bitcast(F32), 0.0).then_inc(xa_cleared, 1)
            nc.vector.memset(low_rows[:, :], 0.0).then_inc(low_rows_set, 1)
            dve.wait_ge(low_rows_set, 1)
            for g in (1, 3):
                nc.vector.memset(low_rows[g * STEP:(g + 1) * STEP, :], -1.0).then_inc(low_rows_set, 1)

            def x1_low(b, slot):
                for h in range(2):
                    dve.wait_ge(x1_hi_ready, 2 * b + h + 1)
                    part = slice(h * HALF, (h + 1) * HALF)
                    nc.vector.tensor_tensor(x1t_lo[slot][:, part], x1_ps[h][:, :],
                                            x1t_hi[slot][:, part].bitcast(F32), ALU.subtract).then_inc(x1_lo_ready, 1)

            groups = xa_parts[:, :].rearrange("p (v g m) -> p v g m", v=2, g=2)

            def finish(b, slot, nth):
                xa = acc[slot][xa_bank[slot]][:, xa_at[slot]:xa_at[slot] + R]
                dve.wait_ge(main_done, b + 1)
                if not is_first(b):
                    dve.wait_ge(xa_turned, b)
                for g in range(2):
                    hi = nc.vector.tensor_copy(groups[:, 0, g, 0:R], xa)
                hi.then_inc(xa_hi_ready, 1)
                dve.wait_ge(xa_hi_ready, b + 1)
                for g in range(2):
                    lo = nc.vector.tensor_tensor(groups[:, 1, g, 0:R], xa, groups[:, 0, g, 0:R].bitcast(F32),
                                                 ALU.subtract)
                lo.then_inc(xa_ready, 1)
                dve.wait_ge(delta_done, b + 1)
                if nth is not None:
                    dve.wait_ge(stored[slot], 16 * nth)
                at, o0, width = output_piece(slot, 2)
                nc.vector.tensor_copy(out_sb[slot][:, o0:o0 + width], acc[slot][2][:, at:at + width]
                                      ).then_inc(out_dve_ready, 1)

            x1_low(0, 0)
            for k in range(K):
                dve.wait_ge(w_hi_ready, k + 1)
                nc.vector.tensor_tensor(w_parts[:, K + k, R:R + O], w_raw[:, k % WST, :],
                                        w_parts[:, k, R:R + O].bitcast(F32), ALU.subtract).then_inc(w_lo_ready, 1)
                if k == 0:
                    dve.wait_ge(a_hi_ready, 1)
                    nc.vector.tensor_tensor(a_parts[:, K:2 * K, :], a_raw[:, :, :],
                                            a_parts[:, 0:K, :].bitcast(F32), ALU.subtract).then_inc(a_lo_ready, 1)
            x1_low(1, 1)
            dve.wait_ge(low_rows_set, 3)
            for a in range(NA):
                dve.wait_ge(b_rounded, a + 1)
                nc.vector.scalar_tensor_tensor(out=b_stack[:, a, :], in0=b_stack[:, a, :].bitcast(F32),
                                               scalar=low_rows[:, 0:1], in1=b_raw[:, a, :],
                                               op0=ALU.mult, op1=ALU.add).then_inc(b_ready, 1)
            dve.wait_ge(xa_cleared, 1)
            finish(0, 0, None)
            x1_low(2, 0)
            finish(1, 1, None)
            x1_low(3, 1)
            with dve.Fori(0, (B - 4) // 2) as i:
                finish(2 * i + 2, 0, i + 1)
                x1_low(2 * i + 4, 0)
                finish(2 * i + 3, 1, i + 1)
                x1_low(2 * i + 5, 1)
            finish(B - 2, 0, B // 2 - 1)
            finish(B - 1, 1, B // 2 - 1)

        @block.gpsimd
        def _(pool):
            def add_identity(b, slot, nth):
                pool.wait_ge(wc_loaded[slot], 16 * (nth + 1))
                nc.gpsimd.tensor_tensor(wc_sb[slot][:, :], wc_sb[slot][:, :], ident[:, :], ALU.add
                                        ).then_inc(wc_ready, 1)

            def place_adapter(b, slot):
                a = pool.value_load(adapter_sb[0:1, bass.ds(b, 1)], min_val=0, max_val=NA - 1)
                nc.gpsimd.tensor_copy(w_parts[:, :, A_COLS[slot]:A_COLS[slot] + R],
                                      a_parts[:, :, bass.ds(a * R, R)]).then_inc(a_slot_ready, 1)

            nc.gpsimd.memset(ident[:, :], 0.0).then_inc(zeros_set, 1)
            pool.wait_ge(zeros_set, 1)
            nc.gpsimd.affine_select(out=ident[:, :], in_=ident[:, :], compare_op=ALU.not_equal, fill=1.0, base=0,
                                    pattern=[[-1, P]], channel_multiplier=1).then_inc(ident_ready, 1)
            pool.wait_ge(ident_ready, 1)
            add_identity(0, 0, 0)
            for k in range(K):
                pool.wait_ge(w_loaded[k], 16)
                eye = w_raw[:, k % WST, k * P:(k + 1) * P]
                nc.gpsimd.tensor_tensor(eye, eye, ident[:, :], ALU.add).then_inc(w_eye_added, 1)
                if k == 0:
                    pool.wait_ge(idx_loaded, 32)
                    pool.wait_ge(a_lo_ready, 1)
                    place_adapter(0, 0)
                    place_adapter(1, 1)
                nc.gpsimd.memset(b_raw[:, k, :], 0.0).then_inc(b_cleared, 1)
            add_identity(1, 1, 0)
            pool.wait_ge(b_loaded, 16 * (P // STEP + 1))
            for a in range(NA):
                nc.gpsimd.tensor_scalar(b_raw[:, a, :], b_raw[:, a, :], scal[:, a:a + 1], None, ALU.mult
                                        ).then_inc(b_scaled, 1)
            with pool.Fori(0, (B - 2) // 2) as i:
                for slot in range(2):
                    b = 2 * i + slot + 2
                    add_identity(b, slot, i + 1)
                    pool.wait_ge(main_done, b - 1)
                    place_adapter(b, slot)


_INS = ["x", "cond", "adapter", "cond_w", "w_t", "a_t", "b_t", "scalings"]


def kernel(x, itok_B_1_198, itok_B_0_6, L0_cond_weights, L1_cond_W, L1_cond_A, L1_cond_Bm, L1_cond_scalings):
    import numpy as np
    from concourse import bacc
    from concourse.bass_utils import run_bass_kernel_spmd

    n_adapters, rank, d_in = L1_cond_A.shape
    laid_out = {
        "x": np.asarray(x),
        "cond": np.asarray(itok_B_1_198).reshape(1, -1),
        "adapter": np.asarray(itok_B_0_6).reshape(1, -1),
        "cond_w": np.asarray(L0_cond_weights),
        "w_t": np.asarray(L1_cond_W).T,
        "a_t": np.asarray(L1_cond_A).reshape(n_adapters * rank, d_in).T,
        "b_t": np.asarray(L1_cond_Bm).transpose(2, 0, 1),
        "scalings": np.asarray(L1_cond_scalings).reshape(1, -1),
    }
    nc = bacc.Bacc("TRN2", target_bir_lowering=False, num_devices=1)
    arrays, aps = {}, []
    for name in _INS:
        a = np.ascontiguousarray(laid_out[name])
        arrays[name + "_dram"] = a
        aps.append(nc.dram_tensor(name + "_dram", a.shape, mybir.dt.from_np(a.dtype), kind="ExternalInput").ap())
    out = nc.dram_tensor("out_dram", x.shape, F32, kind="ExternalOutput").ap()
    bass_cond_then_lora(nc, *aps, out)
    return run_bass_kernel_spmd(nc, [arrays], core_ids=[0]).results[0]["out_dram"]
```

```python
from contextlib import ExitStack

import concourse.bass as bass
from concourse import mybir

F32 = mybir.dt.float32
F32R = mybir.dt.float32r
I32 = mybir.dt.int32
ALU = mybir.AluOpType
ACT = mybir.ActivationFunctionType

P = 128
SLOTS = 2


def bass_cond_then_lora(nc: bass.Bass, x, cond, adapter, cond_w, w_t, a_t, b_t, scalings, out):
    B, C, T = x.shape
    n_cond, _, D = cond_w.shape
    O = w_t.shape[1]
    NA = scalings.shape[1]
    R = b_t.shape[0] // NA
    K = T // P
    HALF = T // 2
    HK = K // 2
    assert C == P and D == P and T == K * P and O == T and R == 16 and NA * R == P and B % 2 == 0

    ROW = R + O + R
    A_COLS = (0, R + O)
    EVEN = ((0, 348), (348, 348), (696, 344))
    ODD = ((R, 348), (R + 348, 348), (R + 696, 344))
    PIECES = (EVEN, ODD)
    STEP = 32
    GROUPS = P // STEP
    B_TURN = 3
    LOW_RANK_AT, LOW_RANK_AT_FIRST = 2, 5

    def output_piece(slot, j):
        first, width = PIECES[slot][j]
        lo, hi = max(first, R), min(first + width, R + O)
        return lo - first, lo - R, hi - lo

    xa_bank = (0, 2)
    xa_at = tuple(A_COLS[s] - PIECES[s][xa_bank[s]][0] for s in range(2))

    with ExitStack() as ctx:
        def sb(name, shape, dt):
            return ctx.enter_context(nc.sbuf_tensor(name, shape, dt))

        def sem(name):
            return ctx.enter_context(nc.semaphore(name))

        x_sb = [sb(f"x_sb{s}", [P, T], F32) for s in range(SLOTS)]
        wc_sb = [sb(f"wc_sb{s}", [P, D], F32) for s in range(SLOTS)]
        x1t_hi = [sb(f"x1t_hi{s}", [P, T], F32R) for s in range(SLOTS)]
        x1t_lo = [sb(f"x1t_lo{s}", [P, T], F32R) for s in range(SLOTS)]
        out_sb = [sb(f"out_sb{s}", [P, O], F32) for s in range(SLOTS)]
        w_parts = sb("w_parts", [P, 2 * K, ROW], F32R)
        a_parts = sb("a_parts", [P, 2 * K, P], F32R)
        a_raw = sb("a_raw", [P, K, P], F32)
        w_raw = sb("w_raw", [P, K, O], F32)
        b_raw = sb("b_raw", [P, O], F32)
        b_parts = sb("b_parts", [P, 2, O], F32R)
        b_stack = sb("b_stack", [P, NA, O], F32R)
        b_scratch = nc.dram_tensor("b_scratch", (2, NA, R, O), F32).ap()
        scal = sb("scal", [P, NA], F32)
        scal_b = [sb(f"scal_b{s}", [P, 1], F32) for s in range(SLOTS)]
        ident = sb("ident", [P, P], F32)
        ident_r = sb("ident_r", [P, P], F32R)
        xa_parts = sb("xa_parts", [P, P], F32R)
        xa_t = sb("xa_t", [P, P], F32R)
        cond_sb = sb("cond_sb", [1, B], I32)
        adapter_sb = sb("adapter_sb", [1, B], I32)

        acc = [[ctx.enter_context(nc.psum_tensor(f"acc{s}_{j}", [P, 512], F32)) for j in range(3)] for s in range(2)]
        x1_ps = [ctx.enter_context(nc.psum_tensor(f"x1_ps{h}", [P, HALF], F32)) for h in range(2)]

        idx_loaded = sem("idx_loaded")
        x_loaded = [sem(f"x_loaded{s}") for s in range(SLOTS)]
        wc_loaded = [sem(f"wc_loaded{s}") for s in range(SLOTS)]
        stored = [sem(f"stored{s}") for s in range(SLOTS)]
        w_loaded = [sem(f"w_loaded{k}") for k in range(K)]
        a_loaded = sem("a_loaded")
        b_loaded = sem("b_loaded")
        scal_loaded = sem("scal_loaded")
        b_parts_saved = sem("b_parts_saved")
        b_stacked = sem("b_stacked")
        zeros_set = sem("zeros_set")
        ident_ready = sem("ident_ready")
        ident_r_ready = sem("ident_r_ready")
        b_cleared = sem("b_cleared")
        w_eye_added = sem("w_eye_added")
        w_hi_ready = sem("w_hi_ready")
        w_lo_ready = sem("w_lo_ready")
        a_hi_ready = sem("a_hi_ready")
        a_lo_ready = sem("a_lo_ready")
        b_hi_ready = sem("b_hi_ready")
        b_lo_ready = sem("b_lo_ready")
        xa_cleared = sem("xa_cleared")
        wc_ready = sem("wc_ready")
        a_slot_ready = sem("a_slot_ready")
        x1_done = sem("x1_done")
        x1_hi_ready = sem("x1_hi_ready")
        x1_lo_ready = sem("x1_lo_ready")
        main_done = sem("main_done")
        xa_hi_ready = sem("xa_hi_ready")
        xa_ready = sem("xa_ready")
        xa_turned = sem("xa_turned")
        xa_t_ready = sem("xa_t_ready")
        delta_done = sem("delta_done")
        out_act_ready = sem("out_act_ready")
        out_dve_ready = sem("out_dve_ready")

        block = ctx.enter_context(nc.Block())

        def is_first(b):
            return isinstance(b, int) and b == 0

        def is_last(b):
            return isinstance(b, int) and b == B - 1

        @block.sync
        def _(sp):
            def load_x(b, slot):
                sp.dma_start(x_sb[slot][:, :], x[bass.ds(b, 1), :, :].rearrange("b c t -> (b c) t")
                             ).then_inc(x_loaded[slot], 16)

            def load_wc(b, slot):
                c = sp.value_load(cond_sb[0:1, bass.ds(b, 1)], min_val=0, max_val=n_cond - 1)
                sp.dma_start(wc_sb[slot][:, :], cond_w[bass.ds(c, 1), :, :].rearrange("s c d -> (s c) d")
                             ).then_inc(wc_loaded[slot], 16)

            sp.dma_start(cond_sb[:, :], cond).then_inc(idx_loaded, 16)
            sp.dma_start(adapter_sb[:, :], adapter).then_inc(idx_loaded, 16)
            sp.dma_start(a_raw[:, :, :], a_t.rearrange("(k p) m -> p k m", p=P)).then_inc(a_loaded, 16)
            load_x(0, 0)
            sp.wait_ge(idx_loaded, 32)
            load_wc(0, 0)
            sp.dma_start(scal[:, :], scalings.to_broadcast([P, NA])).then_inc(scal_loaded, 16)
            for k in range(K):
                sp.dma_start(w_raw[:, k, :], w_t[k * P:(k + 1) * P, :]).then_inc(w_loaded[k], 16)
                if k == B_TURN - 1:
                    sp.dma_start(b_raw[:, :], b_t).then_inc(b_loaded, 16)
            load_x(1, 1)
            load_wc(1, 1)
            sp.wait_ge(b_hi_ready, 1)
            sp.wait_ge(b_lo_ready, 1)
            sp.dma_start(b_scratch.rearrange("v a r o -> (a r) v o"), b_parts[:, :, :].bitcast(F32)).then_inc(b_parts_saved, 16)
            sp.wait_ge(b_parts_saved, 16)
            sp.wait_ge(b_cleared, NA)
            for g in range(GROUPS):
                sp.dma_start(b_stack[g * STEP:g * STEP + R, :, :].bitcast(F32), b_scratch[g % 2].rearrange("a r o -> r a o")
                             ).then_inc(b_stacked, 16)

            def store(b, slot):
                sp.wait_ge(out_act_ready, b + 1)
                sp.wait_ge(out_dve_ready, b + 1)
                sp.dma_start(out[bass.ds(b, 1), :, :].rearrange("b c t -> (b c) t"), out_sb[slot][:, :]
                             ).then_inc(stored[slot], 16)

            def step(b, slot):
                if not is_last(b):
                    sp.wait_ge(x1_done, 2 * b + 2)
                    load_x(b + 2, slot)
                    load_wc(b + 2, slot)
                if not is_first(b):
                    store(b - 1, 1 - slot)

            step(0, 0)
            with sp.Fori(0, (B - 4) // 2) as i:
                step(2 * i + 1, 1)
                step(2 * i + 2, 0)
            step(B - 3, 1)
            store(B - 3, 1)
            store(B - 2, 0)
            store(B - 1, 1)
            for s in range(SLOTS):
                sp.wait_ge(stored[s], 16 * (B // 2))

        @block.tensor
        def _(pe):
            def first_product(b, slot, nth):
                pe.wait_ge(x_loaded[slot], 16 * (nth + 1))
                pe.wait_ge(wc_ready, b + 1)
                for h in range(2):
                    for k in range(HK):
                        t0 = (h * HK + k) * P
                        mm = nc.tensor.matmul(x1_ps[h][:, k * P:(k + 1) * P], x_sb[slot][:, t0:t0 + P],
                                              wc_sb[slot][:, :], start=True, stop=True)
                    mm.then_inc(x1_done, 1)

            def second_product(slot, k):
                t = slice(k * P, (k + 1) * P)
                for lhs, part, first in ((x1t_hi, 0, True), (x1t_hi, K, False), (x1t_lo, 0, False)):
                    for j, (c0, width) in enumerate(PIECES[slot]):
                        mm = nc.tensor.matmul(acc[slot][j][:, 0:width], lhs[slot][:, t],
                                              w_parts[:, part + k, c0:c0 + width],
                                              start=(k == 0 and first), stop=False, skip_group_check=True)
                return mm

            def turn_xa(b):
                pe.wait_ge(xa_ready, b + 1)
                nc.tensor.transpose(x1_ps[0][:, 0:P].bitcast(F32R), xa_parts[:, :], ident_r[:, :]
                                    ).then_inc(xa_turned, 1)

            def low_rank_product(b, slot):
                a = pe.value_load(adapter_sb[0:1, bass.ds(b, 1)], min_val=0, max_val=NA - 1)
                pe.wait_ge(xa_t_ready, b + 1)
                for j in range(3):
                    at, o0, width = output_piece(slot, j)
                    rhs = b_stack[:, bass.ds(a, 1), o0:o0 + width].rearrange("p a o -> p (a o)")
                    mm = nc.tensor.matmul(acc[slot][j][:, at:at + width], xa_t[:, :], rhs,
                                          start=False, stop=True, skip_group_check=True)
                mm.then_inc(delta_done, 1)

            def step(b, slot, nth_next):
                pe.wait_ge(a_slot_ready, b + 1)
                if not (isinstance(b, int) and b < 2):
                    pe.wait_ge(out_act_ready, b - 1)
                    pe.wait_ge(out_dve_ready, b - 1)
                for k in range(K):
                    if k % HK == 0:
                        pe.wait_ge(x1_hi_ready, 2 * b + k // HK + 1)
                        pe.wait_ge(x1_lo_ready, 2 * b + k // HK + 1)
                    if is_first(b):
                        pe.wait_ge(w_hi_ready, k + 1)
                        pe.wait_ge(w_lo_ready, k + 1)
                    mm = second_product(slot, k)
                    if k == 0 and not is_first(b):
                        turn_xa(b - 1)
                    second = isinstance(b, int) and b == 1
                    if k == (LOW_RANK_AT_FIRST if second else LOW_RANK_AT) and not is_first(b):
                        if second:
                            pe.wait_ge(b_stacked, 16 * GROUPS)
                        low_rank_product(b - 1, 1 - slot)
                    if k == HK and not is_last(b):
                        if second:
                            pe.wait_ge(xa_t_ready, b)
                        first_product(b + 1, 1 - slot, nth_next)
                mm.then_inc(main_done, 1)

            pe.wait_ge(idx_loaded, 32)
            first_product(0, 0, 0)
            pe.wait_ge(ident_r_ready, 1)
            step(0, 0, 0)
            step(1, 1, 1)
            with pe.Fori(1, B // 2 - 1) as i:
                step(2 * i, 0, i)
                step(2 * i + 1, 1, i + 1)
            step(B - 2, 0, B // 2 - 1)
            step(B - 1, 1, None)
            turn_xa(B - 1)
            low_rank_product(B - 1, 1)

        @block.scalar
        def _(act):
            act.wait_ge(ident_ready, 1)
            nc.scalar.copy(ident_r[:, :], ident[:, :]).then_inc(ident_r_ready, 1)

            def x1_high(b, slot):
                for h in range(2):
                    act.wait_ge(x1_done, 2 * b + h + 1)
                    nc.scalar.copy(x1t_hi[slot][:, h * HALF:(h + 1) * HALF], x1_ps[h][:, :]).then_inc(x1_hi_ready, 1)

            def finish(b, slot, nth):
                act.wait_ge(xa_turned, b + 1)
                nc.scalar.copy(xa_t[:, :], x1_ps[0][:, 0:P]).then_inc(xa_t_ready, 1)
                act.wait_ge(delta_done, b + 1)
                if nth is not None:
                    act.wait_ge(stored[slot], 16 * nth)
                for j in range(2):
                    at, o0, width = output_piece(slot, j)
                    cp = nc.scalar.copy(out_sb[slot][:, o0:o0 + width], acc[slot][j][:, at:at + width])
                cp.then_inc(out_act_ready, 1)

            act.wait_ge(a_loaded, 16)
            nc.scalar.copy(a_parts[:, 0:K, :], a_raw[:, :, :]).then_inc(a_hi_ready, 1)
            for k in range(K):
                act.wait_ge(w_eye_added, k + 1)
                nc.scalar.copy(w_parts[:, k, R:R + O], w_raw[:, k, :]).then_inc(w_hi_ready, 1)
                if k == 0:
                    x1_high(0, 0)
                if k == B_TURN:
                    act.wait_ge(b_loaded, 16)
                    nc.scalar.copy(b_parts[:, 0, :], b_raw[:, :]).then_inc(b_hi_ready, 1)
            x1_high(1, 1)
            finish(0, 0, None)
            x1_high(2, 0)
            finish(1, 1, None)
            x1_high(3, 1)
            with act.Fori(0, (B - 4) // 2) as i:
                finish(2 * i + 2, 0, i + 1)
                x1_high(2 * i + 4, 0)
                finish(2 * i + 3, 1, i + 1)
                x1_high(2 * i + 5, 1)
            finish(B - 2, 0, B // 2 - 1)
            finish(B - 1, 1, B // 2 - 1)

        @block.vector
        def _(dve):
            nc.vector.memset(xa_parts[:, :].bitcast(F32), 0.0).then_inc(xa_cleared, 1)

            def x1_low(b, slot):
                for h in range(2):
                    dve.wait_ge(x1_hi_ready, 2 * b + h + 1)
                    part = slice(h * HALF, (h + 1) * HALF)
                    nc.vector.tensor_tensor(x1t_lo[slot][:, part], x1_ps[h][:, :],
                                            x1t_hi[slot][:, part].bitcast(F32), ALU.subtract).then_inc(x1_lo_ready, 1)

            groups = xa_parts[:, :].rearrange("p (v g m) -> p v g m", v=2, g=2)

            def finish(b, slot, nth):
                xa = acc[slot][xa_bank[slot]][:, xa_at[slot]:xa_at[slot] + R]
                s_a = scal_b[slot][:, 0:1]
                dve.wait_ge(main_done, b + 1)
                if not is_first(b):
                    dve.wait_ge(xa_turned, b)
                for g in range(2):
                    hi = nc.vector.tensor_scalar(groups[:, 0, g, 0:R], xa, s_a, None, ALU.mult)
                hi.then_inc(xa_hi_ready, 1)
                dve.wait_ge(xa_hi_ready, b + 1)
                for g in range(2):
                    lo = nc.vector.scalar_tensor_tensor(out=groups[:, 1, g, 0:R], in0=xa, scalar=s_a,
                                                        in1=groups[:, 0, g, 0:R].bitcast(F32),
                                                        op0=ALU.mult, op1=ALU.subtract)
                lo.then_inc(xa_ready, 1)
                dve.wait_ge(delta_done, b + 1)
                if nth is not None:
                    dve.wait_ge(stored[slot], 16 * nth)
                at, o0, width = output_piece(slot, 2)
                nc.vector.tensor_copy(out_sb[slot][:, o0:o0 + width], acc[slot][2][:, at:at + width]
                                      ).then_inc(out_dve_ready, 1)

            dve.wait_ge(a_hi_ready, 1)
            nc.vector.tensor_tensor(a_parts[:, K:2 * K, :], a_raw[:, :, :],
                                    a_parts[:, 0:K, :].bitcast(F32), ALU.subtract).then_inc(a_lo_ready, 1)
            for k in range(K):
                dve.wait_ge(w_hi_ready, k + 1)
                nc.vector.tensor_tensor(w_parts[:, K + k, R:R + O], w_raw[:, k, :],
                                        w_parts[:, k, R:R + O].bitcast(F32), ALU.subtract).then_inc(w_lo_ready, 1)
                if k == 0:
                    x1_low(0, 0)
                if k == B_TURN:
                    dve.wait_ge(b_hi_ready, 1)
                    nc.vector.tensor_tensor(b_parts[:, 1, :], b_raw[:, :], b_parts[:, 0, :].bitcast(F32),
                                            ALU.subtract).then_inc(b_lo_ready, 1)
            x1_low(1, 1)
            dve.wait_ge(xa_cleared, 1)
            finish(0, 0, None)
            x1_low(2, 0)
            finish(1, 1, None)
            x1_low(3, 1)
            with dve.Fori(0, (B - 4) // 2) as i:
                finish(2 * i + 2, 0, i + 1)
                x1_low(2 * i + 4, 0)
                finish(2 * i + 3, 1, i + 1)
                x1_low(2 * i + 5, 1)
            finish(B - 2, 0, B // 2 - 1)
            finish(B - 1, 1, B // 2 - 1)

        @block.gpsimd
        def _(pool):
            def add_identity(b, slot, nth):
                pool.wait_ge(wc_loaded[slot], 16 * (nth + 1))
                nc.gpsimd.tensor_tensor(wc_sb[slot][:, :], wc_sb[slot][:, :], ident[:, :], ALU.add
                                        ).then_inc(wc_ready, 1)

            def place_adapter(b, slot):
                a = pool.value_load(adapter_sb[0:1, bass.ds(b, 1)], min_val=0, max_val=NA - 1)
                nc.gpsimd.tensor_copy(scal_b[slot][:, :], scal[:, bass.ds(a, 1)])
                nc.gpsimd.tensor_copy(w_parts[:, :, A_COLS[slot]:A_COLS[slot] + R],
                                      a_parts[:, :, bass.ds(a * R, R)]).then_inc(a_slot_ready, 1)

            nc.gpsimd.memset(ident[:, :], 0.0).then_inc(zeros_set, 1)
            pool.wait_ge(zeros_set, 1)
            nc.gpsimd.affine_select(out=ident[:, :], in_=ident[:, :], compare_op=ALU.not_equal, fill=1.0, base=0,
                                    pattern=[[-1, P]], channel_multiplier=1).then_inc(ident_ready, 1)
            pool.wait_ge(ident_ready, 1)
            add_identity(0, 0, 0)
            pool.wait_ge(idx_loaded, 32)
            pool.wait_ge(scal_loaded, 16)
            pool.wait_ge(a_lo_ready, 1)
            place_adapter(0, 0)
            for k in range(K):
                pool.wait_ge(w_loaded[k], 16)
                eye = w_raw[:, k, k * P:(k + 1) * P]
                nc.gpsimd.tensor_tensor(eye, eye, ident[:, :], ALU.add).then_inc(w_eye_added, 1)
                if k == 0:
                    place_adapter(1, 1)
                nc.gpsimd.memset(b_stack[:, k, :].bitcast(F32), 0.0).then_inc(b_cleared, 1)
            add_identity(1, 1, 0)
            with pool.Fori(0, (B - 2) // 2) as i:
                for slot in range(2):
                    b = 2 * i + slot + 2
                    add_identity(b, slot, i + 1)
                    pool.wait_ge(xa_ready, b - 1)
                    place_adapter(b, slot)


_INS = ["x", "cond", "adapter", "cond_w", "w_t", "a_t", "b_t", "scalings"]


def kernel(x, itok_B_1_198, itok_B_0_6, L0_cond_weights, L1_cond_W, L1_cond_A, L1_cond_Bm, L1_cond_scalings):
    import numpy as np
    from concourse import bacc
    from concourse.bass_utils import run_bass_kernel_spmd

    n_adapters, rank, d_in = L1_cond_A.shape
    laid_out = {
        "x": np.asarray(x),
        "cond": np.asarray(itok_B_1_198).reshape(1, -1),
        "adapter": np.asarray(itok_B_0_6).reshape(1, -1),
        "cond_w": np.asarray(L0_cond_weights),
        "w_t": np.asarray(L1_cond_W).T,
        "a_t": np.asarray(L1_cond_A).reshape(n_adapters * rank, d_in).T,
        "b_t": np.asarray(L1_cond_Bm).transpose(0, 2, 1).reshape(n_adapters * rank, -1),
        "scalings": np.asarray(L1_cond_scalings).reshape(1, -1),
    }
    nc = bacc.Bacc("TRN2", target_bir_lowering=False, num_devices=1)
    arrays, aps = {}, []
    for name in _INS:
        a = np.ascontiguousarray(laid_out[name])
        arrays[name + "_dram"] = a
        aps.append(nc.dram_tensor(name + "_dram", a.shape, mybir.dt.from_np(a.dtype), kind="ExternalInput").ap())
    out = nc.dram_tensor("out_dram", x.shape, F32, kind="ExternalOutput").ap()
    bass_cond_then_lora(nc, *aps, out)
    return run_bass_kernel_spmd(nc, [arrays], core_ids=[0]).results[0]["out_dram"]
```

```python
from contextlib import ExitStack

import concourse.bass as bass
from concourse import mybir

F32 = mybir.dt.float32
F32R = mybir.dt.float32r
I32 = mybir.dt.int32
ALU = mybir.AluOpType

P = 128
SLOTS = 2


def bass_cond_then_lora(nc: bass.Bass, x_t, cond, adapter, cond_w, w_t, a_t, b_t, scalings, out):
    B, _, K, C = x_t.shape
    n_cond, _, D = cond_w.shape
    T, O = w_t.shape
    NA = scalings.shape[1]
    R = b_t.shape[0] // NA
    HALF = O // 2
    assert C == P and D == P and T == K * P and O == T and R == 16 and NA * R == P and B % 2 == 0

    ROW = R + O + R
    A_COLS = (0, R + O)
    PIECES = (((0, 348), (348, 348), (696, 344)), ((R, 348), (R + 348, 348), (R + 696, 344)))
    NP = len(PIECES[0])
    STEP = 32
    GROUPS = P // STEP
    B_TURN = 3
    LOW_RANK_AT, FINAL_AT = 2, 5
    LOW_RANK_AT_FIRST, FINAL_AT_FIRST = 5, 7

    def z_piece(slot, j):
        first, width = PIECES[slot][j]
        lo, hi = max(first, R), min(first + width, R + O)
        return lo - first, lo - R, hi - lo

    XA_BANK = (0, NP - 1)
    XA_AT = tuple(A_COLS[s] - PIECES[s][XA_BANK[s]][0] for s in range(SLOTS))

    with ExitStack() as ctx:
        def sb(name, shape, dt):
            return ctx.enter_context(nc.sbuf_tensor(name, shape, dt))

        def psum(name):
            return ctx.enter_context(nc.psum_tensor(name, [P, 512], F32))

        def sem(name):
            return ctx.enter_context(nc.semaphore(name))

        x_raw = [sb(f"x_raw{s}", [P, K * C], F32) for s in range(SLOTS)]
        x_hi = [sb(f"x_hi{s}", [P, K * C], F32R) for s in range(SLOTS)]
        x_lo = [sb(f"x_lo{s}", [P, K * C], F32R) for s in range(SLOTS)]
        wc_raw = [sb(f"wc_raw{s}", [P, D], F32) for s in range(SLOTS)]
        wc_hi = [sb(f"wc_hi{s}", [P, D], F32R) for s in range(SLOTS)]
        wc_lo = [sb(f"wc_lo{s}", [P, D], F32R) for s in range(SLOTS)]
        scal_b = [sb(f"scal_b{s}", [P, 1], F32) for s in range(SLOTS)]
        out_sb = [sb(f"out_sb{s}", [P, O], F32) for s in range(SLOTS)]
        z_hi = sb("z_hi", [P, O], F32R)
        z_lo = sb("z_lo", [P, O], F32R)
        xa_parts = sb("xa_parts", [P, P], F32R)
        xa_t = sb("xa_t", [P, P], F32R)
        w_parts = sb("w_parts", [P, 2 * K, ROW], F32R)
        a_parts = sb("a_parts", [P, 2 * K, P], F32R)
        a_raw = sb("a_raw", [P, K, P], F32)
        w_raw = sb("w_raw", [P, K, O], F32)
        b_raw = sb("b_raw", [P, O], F32)
        b_parts = sb("b_parts", [P, 2, O], F32R)
        b_stack = sb("b_stack", [P, NA, O], F32R)
        b_scratch = nc.dram_tensor("b_scratch", (2, NA, R, O), F32).ap()
        scal = sb("scal", [P, NA], F32)
        ident = sb("ident", [P, P], F32)
        ident_r = sb("ident_r", [P, P], F32R)
        cond_sb = sb("cond_sb", [1, B], I32)
        adapter_sb = sb("adapter_sb", [1, B], I32)

        z_ps = [[psum(f"z_ps{s}_{j}") for j in range(NP)] for s in range(SLOTS)]
        out_ps = [psum(f"out_ps{h}") for h in range(2)]

        idx_loaded = sem("idx_loaded")
        x_loaded = [sem(f"x_loaded{s}") for s in range(SLOTS)]
        wc_loaded = [sem(f"wc_loaded{s}") for s in range(SLOTS)]
        stored = [sem(f"stored{s}") for s in range(SLOTS)]
        w_loaded = [sem(f"w_loaded{k}") for k in range(K)]
        a_loaded = sem("a_loaded")
        b_loaded = sem("b_loaded")
        scal_loaded = sem("scal_loaded")
        b_parts_saved = sem("b_parts_saved")
        b_stacked = sem("b_stacked")
        zeros_set = sem("zeros_set")
        ident_ready = sem("ident_ready")
        ident_r_ready = sem("ident_r_ready")
        b_cleared = sem("b_cleared")
        xa_cleared = sem("xa_cleared")
        w_eye_added = sem("w_eye_added")
        w_hi_ready = sem("w_hi_ready")
        w_lo_ready = sem("w_lo_ready")
        a_hi_ready = sem("a_hi_ready")
        a_lo_ready = sem("a_lo_ready")
        b_hi_ready = sem("b_hi_ready")
        b_lo_ready = sem("b_lo_ready")
        x_hi_ready = sem("x_hi_ready")
        x_lo_ready = sem("x_lo_ready")
        wc_eye_added = sem("wc_eye_added")
        wc_hi_ready = sem("wc_hi_ready")
        wc_lo_ready = sem("wc_lo_ready")
        a_slot_ready = sem("a_slot_ready")
        main_done = sem("main_done")
        xa_hi_ready = sem("xa_hi_ready")
        xa_ready = sem("xa_ready")
        xa_turned = sem("xa_turned")
        xa_t_ready = sem("xa_t_ready")
        z_done = sem("z_done")
        z_hi_ready = sem("z_hi_ready")
        z_lo_ready = sem("z_lo_ready")
        final_done = sem("final_done")
        out_act_ready = sem("out_act_ready")
        out_dve_ready = sem("out_dve_ready")

        block = ctx.enter_context(nc.Block())

        @block.sync
        def _(sp):
            def load_x(b, slot):
                sp.dma_start(x_raw[slot][:, :], x_t[bass.ds(b, 1), :, :, :].rearrange("b p k c -> (b p) (k c)")
                             ).then_inc(x_loaded[slot], 16)

            def load_wc(b, slot):
                c = sp.value_load(cond_sb[0:1, bass.ds(b, 1)], min_val=0, max_val=n_cond - 1)
                sp.dma_start(wc_raw[slot][:, :], cond_w[bass.ds(c, 1), :, :].rearrange("s c d -> (s c) d")
                             ).then_inc(wc_loaded[slot], 16)

            def store(b, slot):
                sp.wait_ge(out_act_ready, b + 1)
                sp.wait_ge(out_dve_ready, b + 1)
                sp.dma_start(out[bass.ds(b, 1), :, :].rearrange("b c t -> (b c) t"), out_sb[slot][:, :]
                             ).then_inc(stored[slot], 16)

            for k in range(K):
                sp.dma_start(w_raw[:, k, :], w_t[k * P:(k + 1) * P, :]).then_inc(w_loaded[k], 16)
                if k == 0:
                    sp.dma_start(a_raw[:, :, :], a_t.rearrange("(k p) m -> p k m", p=P)).then_inc(a_loaded, 16)
                    sp.dma_start(adapter_sb[:, :], adapter).then_inc(idx_loaded, 16)
                    sp.dma_start(scal[:, :], scalings.to_broadcast([P, NA])).then_inc(scal_loaded, 16)
                    load_x(0, 0)
                    sp.dma_start(cond_sb[:, :], cond).then_inc(idx_loaded, 16)
                if k == B_TURN - 1:
                    sp.dma_start(b_raw[:, :], b_t).then_inc(b_loaded, 16)
            load_x(1, 1)
            sp.wait_ge(idx_loaded, 32)
            load_wc(0, 0)
            load_wc(1, 1)
            sp.wait_ge(b_hi_ready, 1)
            sp.wait_ge(b_lo_ready, 1)
            sp.dma_start(b_scratch.rearrange("v a r o -> (a r) v o"), b_parts[:, :, :].bitcast(F32)
                         ).then_inc(b_parts_saved, 16)
            sp.wait_ge(b_parts_saved, 16)
            sp.wait_ge(b_cleared, NA)
            for g in range(GROUPS):
                sp.dma_start(b_stack[g * STEP:g * STEP + R, :, :].bitcast(F32),
                             b_scratch[g % 2].rearrange("a r o -> r a o")).then_inc(b_stacked, 16)

            def step(b, slot, first=False):
                sp.wait_ge(x_lo_ready, b + 1)
                load_x(b + 2, slot)
                sp.wait_ge(wc_lo_ready, b + 1)
                load_wc(b + 2, slot)
                if not first:
                    store(b - 1, 1 - slot)

            step(0, 0, first=True)
            with sp.Fori(0, (B - 4) // 2) as i:
                step(2 * i + 1, 1)
                step(2 * i + 2, 0)
            step(B - 3, 1)
            store(B - 3, 1)
            store(B - 2, 0)
            for h, ready in enumerate((out_act_ready, out_dve_ready)):
                o = slice(h * HALF, (h + 1) * HALF)
                sp.wait_ge(ready, B)
                sp.dma_start(out[B - 1, :, o], out_sb[1][:, o]).then_inc(stored[1], 16)
            sp.wait_ge(stored[0], 16 * (B // 2))
            sp.wait_ge(stored[1], 16 * (B // 2 + 1))

        @block.tensor
        def _(pe):
            def main_product(slot, k):
                t = slice(k * C, (k + 1) * C)
                for lhs, part, opens in ((x_hi, 0, k == 0), (x_hi, K, False), (x_lo, 0, False)):
                    for j, (c0, width) in enumerate(PIECES[slot]):
                        mm = nc.tensor.matmul(z_ps[slot][j][:, 0:width], lhs[slot][:, t],
                                              w_parts[:, part + k, c0:c0 + width],
                                              start=opens, stop=False, skip_group_check=True)
                return mm

            def turn_xa(b):
                pe.wait_ge(xa_ready, b + 1)
                nc.tensor.transpose(out_ps[0][:, 0:P].bitcast(F32R), xa_parts[:, :], ident_r[:, :]
                                    ).then_inc(xa_turned, 1)

            def low_rank_product(b, slot):
                a = pe.value_load(adapter_sb[0:1, bass.ds(b, 1)], min_val=0, max_val=NA - 1)
                pe.wait_ge(xa_t_ready, b + 1)
                for j in range(NP):
                    at, o0, width = z_piece(slot, j)
                    rhs = b_stack[:, bass.ds(a, 1), o0:o0 + width].rearrange("p a o -> p (a o)")
                    nc.tensor.matmul(z_ps[slot][j][:, at:at + width], xa_t[:, :], rhs,
                                     start=False, stop=True, skip_group_check=True).then_inc(z_done, 1)

            def final_product(b, slot):
                pe.wait_ge(wc_hi_ready, b + 1)
                pe.wait_ge(wc_lo_ready, b + 1)
                for h in range(2):
                    pe.wait_ge(z_lo_ready, NP * b + 2 + h)
                    o = slice(h * HALF, (h + 1) * HALF)
                    nc.tensor.matmul(out_ps[h][:, :], wc_hi[slot][:, :], z_hi[:, o], start=True, stop=False)
                    nc.tensor.matmul(out_ps[h][:, :], wc_hi[slot][:, :], z_lo[:, o], start=False, stop=False)
                    nc.tensor.matmul(out_ps[h][:, :], wc_lo[slot][:, :], z_hi[:, o], start=False, stop=True
                                     ).then_inc(final_done, 1)

            def step(b, slot, nth=None):
                pe.wait_ge(a_slot_ready, b + 1)
                pe.wait_ge(x_hi_ready, b + 1)
                pe.wait_ge(x_lo_ready, b + 1)
                if nth is None:
                    pe.wait_ge(z_lo_ready, NP * (b - 1))
                for k in range(K):
                    if nth == 0:
                        pe.wait_ge(w_hi_ready, k + 1)
                        pe.wait_ge(w_lo_ready, k + 1)
                    mm = main_product(slot, k)
                    if k == K - 1:
                        mm.then_inc(main_done, 1)
                    if nth == 0:
                        continue
                    if k == 0:
                        if nth is None:
                            pe.wait_ge(out_act_ready, b - 1)
                        turn_xa(b - 1)
                    if k == (LOW_RANK_AT if nth is None else LOW_RANK_AT_FIRST):
                        if nth == 1:
                            pe.wait_ge(b_stacked, 16 * GROUPS)
                        low_rank_product(b - 1, 1 - slot)
                    if k == (FINAL_AT if nth is None else FINAL_AT_FIRST):
                        if nth is None:
                            pe.wait_ge(out_dve_ready, b - 1)
                        final_product(b - 1, 1 - slot)

            pe.wait_ge(idx_loaded, 32)
            pe.wait_ge(ident_r_ready, 1)
            step(0, 0, 0)
            step(1, 1, 1)
            with pe.Fori(1, B // 2) as i:
                step(2 * i, 0)
                step(2 * i + 1, 1)
            pe.wait_ge(out_act_ready, B - 1)
            turn_xa(B - 1)
            low_rank_product(B - 1, 1)
            pe.wait_ge(out_dve_ready, B - 1)
            final_product(B - 1, 1)

        @block.scalar
        def _(act):
            def x_high(b, slot, nth):
                act.wait_ge(x_loaded[slot], 16 * (nth + 1))
                nc.scalar.copy(x_hi[slot][:, :], x_raw[slot][:, :]).then_inc(x_hi_ready, 1)

            def wc_high(b, slot):
                act.wait_ge(wc_eye_added, b + 1)
                nc.scalar.copy(wc_hi[slot][:, :], wc_raw[slot][:, :]).then_inc(wc_hi_ready, 1)

            def xa_copy(b):
                act.wait_ge(xa_turned, b + 1)
                nc.scalar.copy(xa_t[:, :], out_ps[0][:, 0:P]).then_inc(xa_t_ready, 1)

            def z_high(b, slot):
                for j in range(NP):
                    at, o0, width = z_piece(slot, j)
                    act.wait_ge(z_done, NP * b + j + 1)
                    nc.scalar.copy(z_hi[:, o0:o0 + width], z_ps[slot][j][:, at:at + width]).then_inc(z_hi_ready, 1)

            def out_half(b, slot, nth):
                act.wait_ge(final_done, 2 * b + 1)
                if nth is not None:
                    act.wait_ge(stored[slot], 16 * nth)
                nc.scalar.copy(out_sb[slot][:, 0:HALF], out_ps[0][:, :]).then_inc(out_act_ready, 1)

            act.wait_ge(ident_ready, 1)
            nc.scalar.copy(ident_r[:, :], ident[:, :]).then_inc(ident_r_ready, 1)
            for k in range(K):
                act.wait_ge(w_eye_added, k + 1)
                nc.scalar.copy(w_parts[:, k, R:R + O], w_raw[:, k, :]).then_inc(w_hi_ready, 1)
                if k == 0:
                    act.wait_ge(a_loaded, 16)
                    nc.scalar.copy(a_parts[:, 0:K, :], a_raw[:, :, :]).then_inc(a_hi_ready, 1)
                    x_high(0, 0, 0)
                if k == B_TURN:
                    act.wait_ge(b_loaded, 16)
                    nc.scalar.copy(b_parts[:, 0, :], b_raw[:, :]).then_inc(b_hi_ready, 1)
            x_high(1, 1, 0)
            wc_high(0, 0)

            def step(b, slot, nth, next_nth):
                xa_copy(b - 1)
                act.wait_ge(main_done, b)
                x_high(b + 1, 1 - slot, next_nth)
                z_high(b - 1, 1 - slot)
                wc_high(b, slot)
                out_half(b - 1, 1 - slot, nth)

            step(1, 1, None, 1)
            step(2, 0, None, 1)
            with act.Fori(1, B // 2 - 1) as i:
                step(2 * i + 1, 1, i, i + 1)
                step(2 * i + 2, 0, i, i + 1)
            xa_copy(B - 2)
            z_high(B - 2, 0)
            wc_high(B - 1, 1)
            out_half(B - 2, 0, B // 2 - 1)
            xa_copy(B - 1)
            z_high(B - 1, 1)
            out_half(B - 1, 1, B // 2 - 1)

        @block.vector
        def _(dve):
            xa_groups = xa_parts[:, :].rearrange("p (v g m) -> p v g m", v=2, g=2)

            def x_low(b, slot):
                dve.wait_ge(x_hi_ready, b + 1)
                nc.vector.tensor_tensor(x_lo[slot][:, :], x_raw[slot][:, :], x_hi[slot][:, :].bitcast(F32),
                                        ALU.subtract).then_inc(x_lo_ready, 1)

            def xa_split(b, slot, first=False):
                xa = z_ps[slot][XA_BANK[slot]][:, XA_AT[slot]:XA_AT[slot] + R]
                s_a = scal_b[slot][:, 0:1]
                dve.wait_ge(main_done, b + 1)
                if not first:
                    dve.wait_ge(xa_turned, b)
                for g in range(2):
                    hi = nc.vector.tensor_scalar(xa_groups[:, 0, g, 0:R], xa, s_a, None, ALU.mult)
                hi.then_inc(xa_hi_ready, 1)
                dve.wait_ge(xa_hi_ready, b + 1)
                for g in range(2):
                    lo = nc.vector.scalar_tensor_tensor(out=xa_groups[:, 1, g, 0:R], in0=xa, scalar=s_a,
                                                        in1=xa_groups[:, 0, g, 0:R].bitcast(F32),
                                                        op0=ALU.mult, op1=ALU.subtract)
                lo.then_inc(xa_ready, 1)

            def z_low(b, slot):
                for j in range(NP):
                    at, o0, width = z_piece(slot, j)
                    dve.wait_ge(z_hi_ready, NP * b + j + 1)
                    nc.vector.tensor_tensor(z_lo[:, o0:o0 + width], z_ps[slot][j][:, at:at + width],
                                            z_hi[:, o0:o0 + width].bitcast(F32), ALU.subtract
                                            ).then_inc(z_lo_ready, 1)

            def out_half(b, slot, nth):
                dve.wait_ge(final_done, 2 * b + 2)
                if nth is not None:
                    dve.wait_ge(stored[slot], 16 * nth)
                nc.vector.tensor_copy(out_sb[slot][:, HALF:O], out_ps[1][:, :]).then_inc(out_dve_ready, 1)

            nc.vector.memset(xa_parts[:, :].bitcast(F32), 0.0).then_inc(xa_cleared, 1)
            for k in range(K):
                dve.wait_ge(w_hi_ready, k + 1)
                nc.vector.tensor_tensor(w_parts[:, K + k, R:R + O], w_raw[:, k, :],
                                        w_parts[:, k, R:R + O].bitcast(F32), ALU.subtract).then_inc(w_lo_ready, 1)
                if k == 0:
                    dve.wait_ge(a_hi_ready, 1)
                    nc.vector.tensor_tensor(a_parts[:, K:2 * K, :], a_raw[:, :, :],
                                            a_parts[:, 0:K, :].bitcast(F32), ALU.subtract).then_inc(a_lo_ready, 1)
                    x_low(0, 0)
                if k == B_TURN:
                    dve.wait_ge(b_hi_ready, 1)
                    nc.vector.tensor_tensor(b_parts[:, 1, :], b_raw[:, :], b_parts[:, 0, :].bitcast(F32),
                                            ALU.subtract).then_inc(b_lo_ready, 1)
            x_low(1, 1)
            dve.wait_ge(xa_cleared, 1)

            def step(b, slot, nth, first=False):
                xa_split(b - 1, 1 - slot, first)
                x_low(b + 1, 1 - slot)
                z_low(b - 1, 1 - slot)
                out_half(b - 1, 1 - slot, nth)

            step(1, 1, None, first=True)
            step(2, 0, None)
            with dve.Fori(1, B // 2 - 1) as i:
                step(2 * i + 1, 1, i)
                step(2 * i + 2, 0, i)
            for b, slot in ((B - 2, 0), (B - 1, 1)):
                xa_split(b, slot)
                z_low(b, slot)
                out_half(b, slot, B // 2 - 1)

        @block.gpsimd
        def _(pool):
            def place_adapter(b, slot):
                a = pool.value_load(adapter_sb[0:1, bass.ds(b, 1)], min_val=0, max_val=NA - 1)
                nc.gpsimd.tensor_copy(scal_b[slot][:, :], scal[:, bass.ds(a, 1)])
                nc.gpsimd.tensor_copy(w_parts[:, :, A_COLS[slot]:A_COLS[slot] + R],
                                      a_parts[:, :, bass.ds(a * R, R)]).then_inc(a_slot_ready, 1)

            def split_wc(b, slot, nth):
                pool.wait_ge(wc_loaded[slot], 16 * (nth + 1))
                nc.gpsimd.tensor_tensor(wc_raw[slot][:, :], wc_raw[slot][:, :], ident[:, :], ALU.add
                                        ).then_inc(wc_eye_added, 1)
                pool.wait_ge(wc_hi_ready, b + 1)
                nc.gpsimd.tensor_tensor(wc_lo[slot][:, :], wc_raw[slot][:, :], wc_hi[slot][:, :].bitcast(F32),
                                        ALU.subtract).then_inc(wc_lo_ready, 1)

            nc.gpsimd.memset(ident[:, :], 0.0).then_inc(zeros_set, 1)
            pool.wait_ge(zeros_set, 1)
            nc.gpsimd.affine_select(out=ident[:, :], in_=ident[:, :], compare_op=ALU.not_equal, fill=1.0, base=0,
                                    pattern=[[-1, P]], channel_multiplier=1).then_inc(ident_ready, 1)
            pool.wait_ge(ident_ready, 1)
            for k in range(K):
                pool.wait_ge(w_loaded[k], 16)
                eye = w_raw[:, k, k * P:(k + 1) * P]
                nc.gpsimd.tensor_tensor(eye, eye, ident[:, :], ALU.add).then_inc(w_eye_added, 1)
                if k == 0:
                    pool.wait_ge(idx_loaded, 32)
                    pool.wait_ge(scal_loaded, 16)
                    pool.wait_ge(a_lo_ready, 1)
                    place_adapter(0, 0)
                if k == K - 1:
                    place_adapter(1, 1)
                nc.gpsimd.memset(b_stack[:, k, :].bitcast(F32), 0.0).then_inc(b_cleared, 1)
            split_wc(0, 0, 0)

            def step(b, slot, nth):
                pool.wait_ge(xa_ready, b)
                place_adapter(b + 1, 1 - slot)
                split_wc(b, slot, nth)

            step(1, 1, 0)
            with pool.Fori(1, B // 2 - 1) as i:
                step(2 * i, 0, i)
                step(2 * i + 1, 1, i)
            step(B - 2, 0, B // 2 - 1)
            split_wc(B - 1, 1, B // 2 - 1)


_INS = ["x_t", "cond", "adapter", "cond_w", "w_t", "a_t", "b_t", "scalings"]


def kernel(x, itok_B_1_198, itok_B_0_6, L0_cond_weights, L1_cond_W, L1_cond_A, L1_cond_Bm, L1_cond_scalings):
    import numpy as np
    from concourse import bacc
    from concourse.bass_utils import run_bass_kernel_spmd

    n_batches, C, T = x.shape
    n_adapters, rank, d_in = L1_cond_A.shape
    laid_out = {
        "x_t": np.asarray(x).reshape(n_batches, C, T // P, P).transpose(0, 3, 2, 1),
        "cond": np.asarray(itok_B_1_198).reshape(1, -1),
        "adapter": np.asarray(itok_B_0_6).reshape(1, -1),
        "cond_w": np.asarray(L0_cond_weights),
        "w_t": np.asarray(L1_cond_W).T,
        "a_t": np.asarray(L1_cond_A).reshape(n_adapters * rank, d_in).T,
        "b_t": np.asarray(L1_cond_Bm).transpose(0, 2, 1).reshape(n_adapters * rank, -1),
        "scalings": np.asarray(L1_cond_scalings).reshape(1, -1),
    }
    nc = bacc.Bacc("TRN2", target_bir_lowering=False, num_devices=1)
    arrays, aps = {}, []
    for name in _INS:
        a = np.ascontiguousarray(laid_out[name])
        arrays[name + "_dram"] = a
        aps.append(nc.dram_tensor(name + "_dram", a.shape, mybir.dt.from_np(a.dtype), kind="ExternalInput").ap())
    out = nc.dram_tensor("out_dram", x.shape, F32, kind="ExternalOutput").ap()
    bass_cond_then_lora(nc, *aps, out)
    return run_bass_kernel_spmd(nc, [arrays], core_ids=[0]).results[0]["out_dram"]
```
